# Optimizing a Trainium2 kernel written in Bass

```python
import numpy as np
import jax
import jax.numpy as jnp

def _softmax(x, axis=-1):
    return jax.nn.softmax(x, axis=axis)

def _gelu(x):
    return jax.nn.gelu(x, approximate=True)

def _silu(x):
    return jax.nn.silu(x)

def _sigmoid(x):
    return jax.nn.sigmoid(x)

def _layernorm(x, axis=-1, eps=1e-05):
    m = jnp.mean(x, axis=axis, keepdims=True)
    v = jnp.var(x, axis=axis, keepdims=True)
    return (x - m) / jnp.sqrt(v + eps)

def _scatter_add(tgt, idx, src, axis=0):
    return tgt.at[idx].add(src)

def _segment_sum(src, seg, n):
    return jax.ops.segment_sum(src, seg, n)
kernel_name = 'mk_adj_preln_d1_adj_r2_fc2140'

def setup_inputs(seed: int=0):
    np.random.seed(seed)
    _w = jnp.asarray

    def _rec_inputs():
        import jax
        import jax.numpy as jnp
        _gk = jax.random.key(seed)
        x = -0.000929 + 1 * jax.random.normal(jax.random.fold_in(_gk, 1), (2048, 256), jnp.float32)
        _a = jax.random.bernoulli(jax.random.fold_in(_gk, 2), 0.0078125, (2048, 2048))
        _af = _a.astype(jnp.float32)
        _af = _af * jax.random.uniform(jax.random.fold_in(_gk, 3), (2048, 2048), jnp.float32, 0.05, 5.22011)
        adj = _af
        return (x, adj)
    x, adj = _rec_inputs()

    def _L0_gnn_setup():
        import jax, jax.numpy as jnp
        import numpy as np
        N = 1024
        HID = 256
        H = 8
        key = jax.random.key(seed)
        ks = jax.random.split(key, 8)
        x = jax.random.normal(ks[0], (N, HID), dtype=jnp.float32)
        sp = jax.random.normal(ks[1], (N, N), dtype=jnp.float32)
        zero_mask = jax.random.uniform(ks[2], (N, N)) < 0.2
        spatial_encoding = jnp.where(zero_mask, 0.0, sp)
        edge_encoding = jax.random.normal(ks[3], (N, N), dtype=jnp.float32)
        s = 1.0 / np.sqrt(HID)
        Wq = jax.random.normal(ks[4], (HID, HID * H), dtype=jnp.float32) * s
        Wk = jax.random.normal(ks[5], (HID, HID * H), dtype=jnp.float32) * s
        Wv = jax.random.normal(ks[6], (HID, HID * H), dtype=jnp.float32) * s
        Wout = jax.random.normal(ks[7], (HID * H, HID), dtype=jnp.float32) * (1.0 / np.sqrt(HID * H))
        return {'x': x, 'spatial_encoding': spatial_encoding, 'edge_encoding': edge_encoding, 'Wq': Wq, 'Wk': Wk, 'Wv': Wv, 'Wout': Wout}
    _L0_gnn_all = _L0_gnn_setup()
    _L0_gnn_in = {k: v for k, v in _L0_gnn_all.items() if k in ('Wq', 'Wk', 'Wv', 'Wout')}
    del _L0_gnn_all
    return {'x': x, 'adj': adj, 'L0_gnn_Wq': _L0_gnn_in['Wq'], 'L0_gnn_Wk': _L0_gnn_in['Wk'], 'L0_gnn_Wv': _L0_gnn_in['Wv'], 'L0_gnn_Wout': _L0_gnn_in['Wout']}

def reference(x, adj, L0_gnn_Wq, L0_gnn_Wk, L0_gnn_Wv, L0_gnn_Wout):
    import jax
    import jax.numpy as jnp

    def _L0_gnn_ref(x, spatial_encoding, edge_encoding, Wq, Wk, Wv, Wout):
        import jax, jax.numpy as jnp
        import numpy as np
        N = 1024
        HID = 256
        H = 8
        n, d = x.shape
        h = Wq.shape[1] // d
        scale = d ** (-0.5)
        q = (x @ Wq).reshape(h, n, d)
        k = (x @ Wk).reshape(h, n, d)
        v = (x @ Wv).reshape(h, n, d)
        a = jnp.einsum('hnd,hmd->hnm', q, k) * scale
        a = a + spatial_encoding + edge_encoding
        mask = spatial_encoding == 0.0
        a = jnp.where(mask, -1000000.0, a)
        a = jax.nn.softmax(a, axis=-1)
        a = jnp.where(mask, 0.0, a)
        out = jnp.einsum('hnm,hmd->hnd', a, v)
        out = out.transpose(1, 0, 2).reshape(n, h * d)
        return out @ Wout
    h = jnp.maximum(_layernorm(x, axis=-1), 0.0)
    x = x + _L0_gnn_ref(h, adj, adj, L0_gnn_Wq, L0_gnn_Wk, L0_gnn_Wv, L0_gnn_Wout)
    return x

_drawn_inputs = setup_inputs


def setup_inputs(seed=0):
    import zlib

    import numpy as np

    out = dict(_drawn_inputs(seed))
    spreads = {}
    factors = {}
    for name, (base, spread) in spreads.items():
        noise = np.random.default_rng([zlib.crc32(name.encode()), seed]).standard_normal(out[name].shape)
        drawn = base * np.exp(spread * noise) if base else spread * noise
        out[name] = jnp.asarray(drawn.astype(out[name].dtype))
    for name, factor in factors.items():
        out[name] = (out[name] * factor).astype(out[name].dtype)
    return out
```

```python
import concourse.bass as bass
from concourse import mybir
from contextlib import ExitStack


def preln_graph_attention(nc, x, adj, wq, wk, wv, wout, out):
    f32, f16, bf16, i32 = mybir.dt.float32, mybir.dt.float16, mybir.dt.bfloat16, mybir.dt.int32
    ALU = mybir.AluOpType
    ACT = mybir.ActivationFunctionType
    AX = mybir.AxisListType
    RED = bass.bass_isa.ReduceOp
    ds = bass.ds

    P = 128
    N, D = x.shape
    H = wq.shape[1] // D
    R = N // H
    KC = D // P
    T = N // P
    CP = H // 2
    BANK = 512
    HALF = N // 2
    XT_GROUPS = KC * N // BANK
    TG = T // 4
    UNITS = 4 * KC * CP
    USES = UNITS + 4 * T
    MASKED = -3.0e38
    REF_MASK = -1.0e6
    P_SCALE = 32768.0
    EPS = 1e-5
    SCALE_INV = float(D) ** 0.5

    adj_t = adj.rearrange("(u r c) m -> c u r m", u=2, c=H)
    x_t = x.rearrange("(u r c) d -> u r c d", u=2, c=H)
    out_t = out.rearrange("(u r c) d -> c u r d", u=2, c=H)
    bias_dram = nc.dram_tensor("bias_dram", [T, P, N], f32, kind="Internal").ap()
    bias_dram_cu = bias_dram.rearrange("(c u) p m -> c u p m", u=2)

    ctx = ExitStack()
    with ctx:
        def sb(name, shape, dt):
            return ctx.enter_context(nc.sbuf_tensor(name, shape, dt))

        def sem(name):
            return ctx.enter_context(nc.semaphore(name))

        w_hi = [sb(f"w{n}_hi", [P, KC, H * D], f16) for n in "qkv"]
        w_lo = [sb(f"w{n}_lo", [P, KC, H * D], f16) for n in "qkv"]
        wo_hi = sb("wo_hi", [P, T, D], f16)
        wo_lo = sb("wo_lo", [P, T, D], f16)
        xT_hi = sb("xT_hi", [P, KC, N], f16)
        xT_lo = sb("xT_lo", [P, KC, N], f16)
        qT = sb("qT", [P, 2, KC, N], f16)
        kT_f = sb("kT", [P, KC * N], f32)
        kT = kT_f.bitcast(f16)[:, :].rearrange("p (s k n) -> p s k n", s=2, k=KC)
        x_nat = kT_f[:, :].rearrange("p (t d) -> p t d", d=D)
        vw_f = sb("vw", [P, T * D], f32)
        vw = vw_f.bitcast(f16)[:, :].rearrange("p (t s d) -> p t s d", s=2, d=D)
        vT = sb("vT", [P, 2, 2, KC, BANK], f16)
        y = sb("y", [P, T, D], f32)
        a = sb("a", [P, 2, N], f32)
        bias = sb("bias", [P, 2, N], f32)
        pt_raw = sb("pt_raw", [P, 2 * N], f32)
        pT = pt_raw.bitcast(f16)[:, 0:2 * N].rearrange("p (s t n) -> p s t n", s=2, n=P)
        raw = pt_raw[:, N:2 * N]
        mask = sb("mask", [P, N], bf16)
        ident = sb("ident", [P, P], f32)
        stats = sb("stats", [P, T, 6], f32)
        mv = sb("mv", [P, T, 2], f32)
        var_e = sb("var_e", [P, T], f32)
        std = sb("std", [P, T], f32)
        rstd = sb("rstd", [P, T], f32)
        newton = sb("newton", [P, T], f32)
        wmax = sb("wmax", [P, 4], f32)
        wall = sb("wall", [P, 4], f32)
        wscale = sb("wscale", [P, 4], f32)
        s_score = sb("s_score", [P, 1], f32)
        s_bias = sb("s_bias", [P, 1], f32)
        kappa = sb("kappa", [P, 1], f32)
        neg_kappa = sb("neg_kappa", [P, 1], f32)
        floor0 = sb("floor0", [P, 1], f32)
        s_out = sb("s_out", [P, 1], f32)
        s_out_inv = sb("s_out_inv", [P, 1], f32)
        ref_mask = sb("ref_mask", [P, 1], f32)
        n_masked = sb("n_masked", [P, T], f32)
        floor_a = sb("floor_a", [P, T], f32)
        floor = sb("floor", [P, T], f32)
        half_max = sb("half_max", [P, 2, 2], f32)
        row_max = sb("row_max", [P, 2], f32)
        shift = sb("shift", [P, 2], f32)
        row_sum = sb("row_sum", [P, 2], f32)
        mask_exp = sb("mask_exp", [P, 2], f32)
        denom = sb("denom", [P, 2], f32)
        rdenom = sb("rdenom", [P, 2], f32)

        stage = [vw_f[:, :], a[:, :, :].rearrange("p u n -> p (u n)"),
                 bias[:, :, :].rearrange("p u n -> p (u n)"), pt_raw[:, :]]
        split_hi = [w[:, :, :].rearrange("p k n -> p (k n)") for w in w_hi] + [wo_hi[:, :, :].rearrange("p t d -> p (t d)")]
        split_lo = [w[:, :, :].rearrange("p k n -> p (k n)") for w in w_lo] + [wo_lo[:, :, :].rearrange("p t d -> p (t d)")]

        work = ctx.enter_context(nc.psum_tensor("work", [P, 4, BANK], f32))
        turn = ctx.enter_context(nc.psum_tensor("turn", [P, 2, BANK], f32))
        yps = ctx.enter_context(nc.psum_tensor("yps", [P, 2, BANK], f32))

        x_loaded = sem("x_loaded")
        w_loaded = [sem(f"w_loaded{n}") for n in "qkvo"]
        xres_loaded = sem("xres_loaded")
        ident_set = sem("ident_set")
        wmax_ready = sem("wmax_ready")
        wall_ready = sem("wall_ready")
        wscale_ready = sem("wscale_ready")
        w_hi_ready = sem("w_hi_ready")
        w_split = sem("w_split")
        small = sem("small")
        var_ready = sem("var_ready")
        std_ready = sem("std_ready")
        x_normed = sem("x_normed")
        bank_filled = sem("bank_filled")
        bank_free = sem("bank_free")
        unit_hi = sem("unit_hi")
        turned = sem("turned")
        turn_hi = sem("turn_hi")
        turn_free = sem("turn_free")
        shift_ready = sem("shift_ready")
        bias_used = sem("bias_used")
        p_ready = sem("p_ready")
        denom_ready = sem("denom_ready")
        y_filled = sem("y_filled")
        y_free = sem("y_free")
        y_chain = sem("y_chain")
        y_final = sem("y_final")
        raw_loaded = sem("raw_loaded")
        mask_made = sem("mask_made")
        adj_scaled = sem("adj_scaled")
        bias_made = sem("bias_made")
        floor_made = sem("floor_made")
        bias_stored = [sem(f"bias_stored{u}") for u in range(2)]
        bias_loaded = [sem(f"bias_loaded{u}") for u in range(2)]
        out_stored = sem("out_stored")

        VF = [("V", 0), ("V", 1), ("F", 0), ("V", 2), ("F", 1), ("V", 3), ("F", 2), ("F", 3)]
        QK_UNITS = 2 * KC * CP

        block = ctx.enter_context(nc.Block())

        @block.sync
        def _(sp):
            sp.dma_start(x_nat, x.rearrange("(t p) d -> p t d", p=P)).then_inc(x_loaded, 16)
            for n, w in enumerate((wq, wk, wv)):
                sp.dma_start(stage[n].rearrange("p (k n) -> p k n", k=KC),
                             w.rearrange("(k p) n -> p k n", p=P)).then_inc(w_loaded[n], 16)
            sp.dma_start(stage[3].rearrange("p (t d) -> p t d", d=D),
                         wout.rearrange("(t p) d -> p t d", p=P)).then_inc(w_loaded[3], 16)
            for u in range(2):
                sp.dma_start(y[:, u:T:2, :], x_t[u]).then_inc(xres_loaded, 16)

            sp.wait_ge(w_split, 4)
            sp.dma_start(raw, adj_t[0, 0]).then_inc(raw_loaded, 16)
            sp.wait_ge(mask_made, 1)
            sp.wait_ge(adj_scaled, 1)
            sp.dma_start(raw, adj_t[0, 1]).then_inc(raw_loaded, 16)
            with sp.Fori(1, T // 2) as i:
                for u in range(2):
                    sp.wait_ge(mask_made, 2 * i + u)
                    sp.wait_ge(adj_scaled, 2 * i + u)
                    sp.dma_start(raw, adj_t[ds(i, 1), u].rearrange("o r m -> (o r) m")).then_inc(raw_loaded, 16)

            for u in range(2):
                sp.wait_ge(bias_stored[u], 16 * (T // 2))
            with sp.Fori(1, H) as h:
                with sp.Fori(0, T // 2) as i:
                    for u in range(2):
                        sp.wait_ge(bias_used, T * h + 2 * i + u - 1)
                        sp.dma_start(bias[:, u, :], bias_dram_cu[ds(i, 1), u].rearrange("o p m -> (o p) m")
                                     ).then_inc(bias_loaded[u], 16)

        @block.gpsimd
        def _(pool):
            pool.memset(ident[:, :], 0.0).then_inc(ident_set, 1)
            pool.memset(ref_mask[:, :], REF_MASK).then_inc(ident_set, 1)
            pool.wait_ge(ident_set, 2)
            pool.affine_select(out=ident[:, :], in_=ident[:, :], compare_op=ALU.not_equal, fill=1.0, base=0,
                               pattern=[[-1, P]], channel_multiplier=1).then_inc(ident_set, 1)
            for n in range(4):
                pool.wait_ge(wmax_ready, n + 1)
                pool.partition_all_reduce(wall[:, n:n + 1], wmax[:, n:n + 1], P, RED.max).then_inc(wall_ready, 1)
            with pool.Fori(0, T // 2) as i:
                for u in range(2):
                    pool.wait_ge(bias_made, 2 * i + u + 1)
                    pool.dma_start(bias_dram_cu[ds(i, 1), u].rearrange("o p m -> (o p) m"),
                                   bias[:, u, :]).then_inc(bias_stored[u], 16)
            for u in range(2):
                pool.wait_ge(bias_stored[u], 16 * (T // 2))

        @block.tensor
        def _(pe):
            pe.wait_ge(ident_set, 3)
            for q in range(N // BANK):
                for k in range(KC):
                    n = KC * q + k
                    pe.wait_ge(x_normed, 4 * q + 4)
                    pe.wait_ge(turn_free, n + 1)
                    for j in range(4):
                        last = pe.transpose(turn[:, n % 2, P * j:P * j + P], x_nat[:, 4 * q + j, P * k:P * k + P],
                                            ident[:, :])
                    last.then_inc(turned, 1)

            def project(bank, w, d0, x0):
                for cc in range(2):
                    o = work[:, bank, R * cc:R * cc + R]
                    for k in range(KC):
                        hi = w_hi[w][:, k, ds(d0 + D * cc, P)]
                        lo = w_lo[w][:, k, ds(d0 + D * cc, P)]
                        pe.matmul(o, hi, xT_hi[:, k, ds(x0, R)], start=(k == 0), stop=False)
                        pe.matmul(o, hi, xT_lo[:, k, ds(x0, R)], start=False, stop=False)
                        last = pe.matmul(o, lo, xT_hi[:, k, ds(x0, R)], start=False, stop=(k == KC - 1))
                last.then_inc(bank_filled, 1)

            def fold(bank, slot, pair, w0):
                for m in range(2):
                    o = work[:, bank, D * m:D * m + D]
                    c0 = P * (2 * pair + m)
                    for k in range(KC):
                        hi = vT[:, slot, 0, k, c0:c0 + P]
                        lo = vT[:, slot, 1, k, c0:c0 + P]
                        whi = wo_hi[:, ds(w0 + k, 1), :].rearrange("p o d -> p (o d)")
                        wlo = wo_lo[:, ds(w0 + k, 1), :].rearrange("p o d -> p (o d)")
                        pe.matmul(o, hi, whi, start=(k == 0), stop=False)
                        pe.matmul(o, hi, wlo, start=False, stop=False)
                        last = pe.matmul(o, lo, whi, start=False, stop=(k == KC - 1))
                last.then_inc(bank_filled, 1)

            def scores(h, t, half):
                use = USES * h + UNITS + 4 * t + 2 * half
                pe.wait_ge(bank_free, use + 2)
                for b in range(2):
                    o = work[:, 2 * half + b, :]
                    cols = slice(HALF * half + BANK * b, HALF * half + BANK * b + BANK)
                    for k in range(KC):
                        hi, lo = qT[:, 0, k, ds(P * t, P)], qT[:, 1, k, ds(P * t, P)]
                        pe.matmul(o, hi, kT[:, 0, k, cols], start=(k == 0), stop=False)
                        pe.matmul(o, hi, kT[:, 1, k, cols], start=False, stop=False)
                        last = pe.matmul(o, lo, kT[:, 0, k, cols], start=False, stop=(k == KC - 1))
                    last.then_inc(bank_filled, 1)

            def transposes(h, t, u, j0):
                g = T * h + t
                if j0 == 0:
                    pe.wait_ge(p_ready, g + 1)
                for j in range(j0, j0 + 2):
                    pe.wait_ge(turn_free, XT_GROUPS + TG * g + j + 1)
                    for b in range(4):
                        last = pe.transpose(turn[:, j % 2, P * b:P * b + P],
                                            a[:, u, BANK * j + P * b:BANK * j + P * b + P], ident[:, :])
                    last.then_inc(turned, 1)

            def apply(h, t, u):
                g = T * h + t
                pe.wait_ge(y_free, g + 1)
                for j in range(TG):
                    pe.wait_ge(turn_free, XT_GROUPS + TG * g + j + 3)
                    for m in range(4 * j, 4 * j + 4):
                        pe.matmul(yps[:, u, :], pT[:, 0, m, :], vw[:, m, :, :].rearrange("p s d -> p (s d)"),
                                  start=(m == 0), stop=False)
                        last = pe.matmul(yps[:, u, D:2 * D], pT[:, 1, m, :], vw[:, m, 0, :],
                                         start=False, stop=(m == T - 1))
                last.then_inc(y_filled, 1)

            def head(h):
                base = USES * h
                with pe.Fori(0, CP) as cp:
                    for w in range(2):
                        for dc in range(KC):
                            n = KC * w + dc
                            pe.wait_ge(bank_free, base + 4 * cp + n + 1)
                            project(n, w, 2 * D * cp + P * dc, R * h)
                use = base + QK_UNITS
                pos = {}
                for n, (kind, cp) in enumerate(VF):
                    pos[kind, cp] = 2 * n
                    for s in range(2):
                        i = 2 * n + s
                        pe.wait_ge(bank_free, use + i + 1)
                        if kind == "F":
                            pe.wait_ge(bank_free, use + pos["V", cp] + 2 + 4)
                        if kind == "V":
                            project(i % 4, 2, 2 * D * cp + P * s, R * h)
                        else:
                            fold(i % 4, cp % 2, s, KC * h)
                scores(h, 0, 0)
                scores(h, 0, 1)
                with pe.Fori(0, T // 2 - 1) as i:
                    for u in range(2):
                        tile_step(h, 2 * i + u, u)
                tile_step(h, T - 2, 0)
                transposes(h, T - 1, 1, 0)
                transposes(h, T - 1, 1, 2)
                apply(h, T - 1, 1)

            def tile_step(h, t, u):
                scores(h, t + 1, 0)
                transposes(h, t, u, 0)
                scores(h, t + 1, 1)
                transposes(h, t, u, 2)
                apply(h, t, u)

            pe.wait_ge(w_split, 4)
            pe.wait_ge(turn_free, XT_GROUPS + 2)
            head(0)
            with pe.Fori(1, H) as h:
                head(h)

        @block.scalar
        def _(act):
            act.wait_ge(var_ready, 1)
            act.activation(std[:, :], var_e[:, :], ACT.Sqrt).then_inc(std_ready, 1)
            for n in range(4):
                act.wait_ge(wscale_ready, n + 1)
                act.activation(split_hi[n], stage[n], ACT.Copy, scale=wscale[:, n:n + 1]).then_inc(w_hi_ready, 1)
                if n == 0:
                    for g in range(XT_GROUPS):
                        q, k = g // KC, g % KC
                        act.wait_ge(turned, g + 1)
                        act.activation(xT_hi[:, k, BANK * q:BANK * q + BANK], turn[:, g % 2, :], ACT.Relu
                                       ).then_inc(turn_hi, 1)

            def bias_tile(t, u, i=None):
                act.wait_ge(raw_loaded, 16 * (t + 1))
                if i is not None:
                    act.wait_ge(bias_stored[u], 16 * i + 16)
                    act.wait_ge(bias_used, t - 1)
                act.activation(bias[:, u, :].rearrange("p (c r) -> p c r", c=H),
                               raw.rearrange("p (r c) -> p c r", c=H), ACT.Copy,
                               scale=s_bias[:, 0:1]).then_inc(adj_scaled, 1)

            def unit(use, n, dst, bank, scale):
                act.wait_ge(bank_filled, use + 1)
                act.activation(dst, bank, ACT.Copy, scale=scale).then_inc(unit_hi, 1)

            def split_p(h, t, j0):
                g = T * h + t
                for j in range(j0, j0 + 2):
                    act.wait_ge(turned, XT_GROUPS + TG * g + j + 1)
                    act.activation(pT[:, 0, 4 * j:4 * j + 4, :].rearrange("p t n -> p (t n)"), turn[:, j % 2, :],
                                   ACT.Copy, scale=P_SCALE).then_inc(turn_hi, 1)

            def exp(h, t, u):
                g = T * h + t
                act.wait_ge(shift_ready, g + 1)
                act.activation(a[:, u, :], a[:, u, :], ACT.Exp, bias=shift[:, u:u + 1], scale=kappa[:, 0:1],
                               accum_out=row_sum[:, u:u + 1]).then_inc(p_ready, 1)
                act.activation(mask_exp[:, u:u + 1], shift[:, u:u + 1], ACT.Exp, bias=ref_mask[:, 0:1],
                               scale=1.0).then_inc(denom_ready, 1)

            def head(h, first):
                base = USES * h
                with act.Fori(0, CP) as cp:
                    for w, dst in ((0, qT), (1, kT)):
                        for dc in range(KC):
                            n = KC * w + dc
                            unit(base + 4 * cp + n, n, dst[:, 0, dc, ds(BANK * cp, BANK)], work[:, n, :], 1.0)
                if first:
                    bias_tile(0, 0)
                use = base + QK_UNITS
                for n, (kind, cp) in enumerate(VF):
                    for s in range(2):
                        i = 2 * n + s
                        if kind == "V":
                            unit(use + i, i, vT[:, cp % 2, 0, s, :], work[:, i % 4, :], 1.0)
                        else:
                            t0 = 4 * cp + 2 * s
                            unit(use + i, i, vw[:, t0:t0 + 2, 0, :],
                                 work[:, i % 4, :].rearrange("p (t d) -> p t d", d=D), 1.0 / P_SCALE)
                if first:
                    bias_tile(1, 1)
                exp(h, 0, 0)
                with act.Fori(0, T // 2 - 1) as i:
                    for u in range(2):
                        split_p(h, 2 * i + u, 0)
                        split_p(h, 2 * i + u, 2)
                        exp(h, 2 * i + u + 1, 1 - u)
                        if first:
                            bias_tile(2 * i + u + 2, u, i)
                split_p(h, T - 2, 0)
                split_p(h, T - 2, 2)
                exp(h, T - 1, 1)
                split_p(h, T - 1, 0)
                split_p(h, T - 1, 2)

            act.wait_ge(small, SMALL_SCALES)
            head(0, True)
            with act.Fori(1, H) as h:
                head(h, False)

            with act.Fori(0, T // 2) as i:
                for u in range(2):
                    act.wait_ge(y_final, 2 * i + u + 1)
                    act.dma_start(out_t[ds(i, 1), u].rearrange("o r d -> (o r) d"),
                                  y[:, ds(2 * i + u, 1), :].rearrange("p o d -> p (o d)")).then_inc(out_stored, 16)
            act.wait_ge(out_stored, 16 * T)

        @block.vector
        def _(dve):
            dve.nop().then_inc(bank_free, 4)
            dve.nop().then_inc(turn_free, 2)
            dve.nop().then_inc(y_free, 2)
            chain = [0]

            def link(ins):
                chain[0] += 1
                ins.then_inc(small, 1)
                dve.wait_ge(small, chain[0])

            dve.wait_ge(x_loaded, 16)
            for t in range(T):
                last = dve.bn_stats(stats[:, t, :], x_nat[:, t, :])
            link(last)
            for t in range(T):
                last = dve.bn_aggr(mv[:, t, :], stats[:, t, :])
            link(last)
            dve.tensor_scalar(var_e[:, :], mv[:, :, 1], EPS, None, ALU.add).then_inc(var_ready, 1)
            dve.wait_ge(w_loaded[0], 16)
            dve.tensor_reduce(wmax[:, 0:1], stage[0], AX.X, ALU.max, apply_absolute_value=True).then_inc(wmax_ready, 1)
            dve.wait_ge(std_ready, 1)
            link(dve.reciprocal(rstd[:, :], std[:, :]))
            link(dve.tensor_tensor(newton[:, :], rstd[:, :], rstd[:, :], ALU.mult))
            link(dve.tensor_tensor(newton[:, :], newton[:, :], var_e[:, :], ALU.mult))
            link(dve.tensor_scalar(newton[:, :], newton[:, :], -0.5, 1.5, ALU.mult, ALU.add))
            link(dve.tensor_tensor(rstd[:, :], rstd[:, :], newton[:, :], ALU.mult))
            for t in range(T):
                dve.tensor_scalar(x_nat[:, t, :], x_nat[:, t, :], mv[:, t, 0:1], rstd[:, t:t + 1],
                                  ALU.subtract, ALU.mult).then_inc(x_normed, 1)

            def scale_of(n, least):
                dve.wait_ge(wall_ready, n + 1)
                s = wscale[:, n:n + 1]
                link(dve.tensor_scalar(s, wall[:, n:n + 1], least, None, ALU.max))
                link(dve.tensor_scalar(s.bitcast(i32), s.bitcast(i32), 0x7f800000, None, ALU.bitwise_and))
                link(dve.reciprocal(s, s))
                dve.tensor_scalar(s, s, 64.0, None, ALU.mult).then_inc(wscale_ready, 1)

            def split_w(n):
                dve.wait_ge(w_hi_ready, n + 1)
                dve.wait_ge(wscale_ready, n + 1)
                dve.scalar_tensor_tensor(out=split_lo[n], in0=stage[n], scalar=wscale[:, n:n + 1], in1=split_hi[n],
                                         op0=ALU.mult, op1=ALU.subtract).then_inc(w_split, 1)

            LEAST = [2.0 ** -20, 2.0 ** -20, 2.0 ** -30, 2.0 ** -30]
            scale_of(0, LEAST[0])
            split_w(0)
            for g in range(XT_GROUPS):
                q, k = g // KC, g % KC
                dve.wait_ge(turn_hi, g + 1)
                dve.scalar_tensor_tensor(out=xT_lo[:, k, BANK * q:BANK * q + BANK], in0=turn[:, g % 2, :], scalar=0.0,
                                         in1=xT_hi[:, k, BANK * q:BANK * q + BANK], op0=ALU.max, op1=ALU.subtract
                                         ).then_inc(turn_free, 1)
            for n in range(1, 4):
                dve.wait_ge(w_loaded[n], 16)
                dve.tensor_reduce(wmax[:, n:n + 1], stage[n], AX.X, ALU.max, apply_absolute_value=True
                                  ).then_inc(wmax_ready, 1)
            for n in range(1, 4):
                scale_of(n, LEAST[n])
            dve.wait_ge(wscale_ready, 4)
            link(dve.tensor_tensor(s_score[:, :], wscale[:, 0:1], wscale[:, 1:2], ALU.mult))
            link(dve.tensor_scalar(s_score[:, :], s_score[:, :], SCALE_INV, None, ALU.mult))
            link(dve.tensor_scalar(s_bias[:, :], s_score[:, :], 2.0, None, ALU.mult))
            link(dve.tensor_scalar(floor0[:, :], s_score[:, :], REF_MASK, None, ALU.mult))
            link(dve.reciprocal(kappa[:, :], s_score[:, :]))
            link(dve.tensor_scalar(neg_kappa[:, :], kappa[:, :], -1.0, None, ALU.mult))
            link(dve.tensor_tensor(s_out[:, :], wscale[:, 2:3], wscale[:, 3:4], ALU.mult))
            link(dve.reciprocal(s_out_inv[:, :], s_out[:, :]))
            assert chain[0] == SMALL_SCALES
            for n in range(1, 4):
                split_w(n)
            dve.wait_ge(xres_loaded, 32)
            yf = y[:, :, :].rearrange("p t d -> p (t d)")
            dve.tensor_scalar(yf, yf, s_out[:, 0:1], None, ALU.mult).then_inc(y_chain, 1)

            def bias_tile(t, u):
                dve.wait_ge(raw_loaded, 16 * (t + 1))
                if not (isinstance(t, int) and t == 0):
                    dve.wait_ge(bias_made, t)
                col = ds(t, 1)
                dve.tensor_scalar(mask[:, :], raw, 0.0, 0.0, ALU.is_equal, ALU.add, accum_out=n_masked[:, col]
                                  ).then_inc(mask_made, 1)
                dve.wait_ge(mask_made, t + 1)
                dve.wait_ge(adj_scaled, t + 1)
                dve.scalar_tensor_tensor(out=bias[:, u, :].rearrange("p (c r) -> p c r", c=H),
                                         in0=mask[:, :].rearrange("p (r c) -> p c r", c=H), scalar=MASKED,
                                         in1=bias[:, u, :].rearrange("p (c r) -> p c r", c=H),
                                         op0=ALU.mult, op1=ALU.add).then_inc(bias_made, 1)
                dve.tensor_scalar(floor_a[:, col], n_masked[:, col], 0.0, MASKED, ALU.is_equal, ALU.mult
                                  ).then_inc(floor_made, 1)
                dve.wait_ge(floor_made, 2 * t + 1)
                dve.tensor_scalar(floor[:, col], floor_a[:, col], floor0[:, 0:1], None, ALU.add
                                  ).then_inc(floor_made, 1)

            def unit(use, count, dst, bank, hi, scale):
                dve.wait_ge(unit_hi, count)
                if scale == 1.0:
                    dve.tensor_tensor(dst, bank, hi, ALU.subtract).then_inc(bank_free, 1)
                else:
                    dve.scalar_tensor_tensor(out=dst, in0=bank, scalar=scale, in1=hi, op0=ALU.mult,
                                             op1=ALU.subtract).then_inc(bank_free, 1)

            def add_bias(h, t, u, half, first, pair):
                use = USES * h + UNITS + 4 * t + 2 * half
                dve.wait_ge(bank_filled, use + 2)
                if half == 0:
                    if first:
                        dve.wait_ge(bias_made, t + 1)
                        dve.wait_ge(floor_made, 2 * t + 2)
                    else:
                        dve.wait_ge(bias_loaded[u], 16 * (T // 2) * (h - 1) + 16 * pair + 16)
                cols = slice(HALF * half, HALF * half + HALF)
                dve.tensor_tensor_reduce(a[:, u, cols], work[:, 2 * half:2 * half + 2, :].rearrange("p b n -> p (b n)"),
                                         bias[:, u, cols], 1.0, MASKED, ALU.add, ALU.max,
                                         half_max[:, u, half:half + 1]).then_inc(bank_free, 2)

            def row_shift(h, t, u):
                g = T * h + t
                dve.wait_ge(bank_free, USES * h + UNITS + 4 * t + 4 + 4)
                dve.tensor_scalar(row_max[:, u:u + 1], half_max[:, u, 0:1], half_max[:, u, 1:2],
                                  floor[:, ds(t, 1)], ALU.max, ALU.max).then_inc(bias_used, 1)
                dve.wait_ge(bias_used, g + 1)
                dve.tensor_scalar(shift[:, u:u + 1], row_max[:, u:u + 1], neg_kappa[:, 0:1], None, ALU.mult
                                  ).then_inc(shift_ready, 1)

            def split_p(h, t, j0):
                g = T * h + t
                for j in range(j0, j0 + 2):
                    dve.wait_ge(turn_hi, XT_GROUPS + TG * g + j + 1)
                    dve.scalar_tensor_tensor(out=pT[:, 1, 4 * j:4 * j + 4, :].rearrange("p t n -> p (t n)"),
                                             in0=turn[:, j % 2, :], scalar=P_SCALE,
                                             in1=pT[:, 0, 4 * j:4 * j + 4, :].rearrange("p t n -> p (t n)"),
                                             op0=ALU.mult, op1=ALU.subtract).then_inc(turn_free, 1)

            def update_y(h, t, u, last):
                g = T * h + t
                dve.wait_ge(denom_ready, g + 1)
                dve.scalar_tensor_tensor(out=denom[:, u:u + 1], in0=mask_exp[:, u:u + 1], scalar=n_masked[:, ds(t, 1)],
                                         in1=row_sum[:, u:u + 1], op0=ALU.mult, op1=ALU.add).then_inc(y_chain, 1)
                dve.wait_ge(y_chain, 3 * g + 2)
                dve.reciprocal(rdenom[:, u:u + 1], denom[:, u:u + 1]).then_inc(y_chain, 1)
                yt = y[:, ds(t, 1), :].rearrange("p o d -> p (o d)")
                dve.wait_ge(y_chain, 3 * g + 3)
                dve.wait_ge(y_filled, g + 1)
                dve.scalar_tensor_tensor(out=yt, in0=yps[:, u, 0:D], scalar=rdenom[:, u:u + 1], in1=yt,
                                         op0=ALU.mult, op1=ALU.add).then_inc(y_chain, 1)
                dve.wait_ge(y_chain, 3 * g + 4)
                dve.scalar_tensor_tensor(out=yt, in0=yps[:, u, D:2 * D], scalar=rdenom[:, u:u + 1], in1=yt,
                                         op0=ALU.mult, op1=ALU.add).then_inc(y_free, 1)

            def head(h, first):
                base = USES * h
                hi0 = UNITS * h
                with dve.Fori(0, CP) as cp:
                    for w, dst in ((0, qT), (1, kT)):
                        for dc in range(KC):
                            n = KC * w + dc
                            cols = ds(BANK * cp, BANK)
                            unit(base + 4 * cp + n, hi0 + 4 * cp + n + 1, dst[:, 1, dc, cols], work[:, n, :],
                                 dst[:, 0, dc, cols], 1.0)
                if first:
                    bias_tile(0, 0)
                use = base + QK_UNITS
                for n, (kind, cp) in enumerate(VF):
                    for s in range(2):
                        i = 2 * n + s
                        count = hi0 + QK_UNITS + i + 1
                        if kind == "V":
                            unit(use + i, count, vT[:, cp % 2, 1, s, :], work[:, i % 4, :], vT[:, cp % 2, 0, s, :], 1.0)
                        else:
                            t0 = 4 * cp + 2 * s
                            unit(use + i, count, vw[:, t0:t0 + 2, 1, :],
                                 work[:, i % 4, :].rearrange("p (t d) -> p t d", d=D), vw[:, t0:t0 + 2, 0, :],
                                 1.0 / P_SCALE)
                if first:
                    bias_tile(1, 1)
                add_bias(h, 0, 0, 0, first, 0)
                add_bias(h, 0, 0, 1, first, 0)
                row_shift(h, 0, 0)
                with dve.Fori(0, T // 2 - 1) as i:
                    for u in range(2):
                        t = 2 * i + u
                        add_bias(h, t + 1, 1 - u, 0, first, i + u)
                        split_p(h, t, 0)
                        add_bias(h, t + 1, 1 - u, 1, first, i + u)
                        row_shift(h, t + 1, 1 - u)
                        split_p(h, t, 2)
                        update_y(h, t, u, False)
                        if first:
                            bias_tile(t + 2, u)
                add_bias(h, T - 1, 1, 0, first, T // 2 - 1)
                split_p(h, T - 2, 0)
                add_bias(h, T - 1, 1, 1, first, T // 2 - 1)
                row_shift(h, T - 1, 1)
                split_p(h, T - 2, 2)
                update_y(h, T - 2, 0, False)
                split_p(h, T - 1, 0)
                split_p(h, T - 1, 2)
                update_y(h, T - 1, 1, False)

            head(0, True)
            with dve.Fori(1, H) as h:
                head(h, False)
            dve.wait_ge(y_free, H * T + 2)
            for t in range(T):
                dve.tensor_scalar(y[:, t, :], y[:, t, :], s_out_inv[:, 0:1], None, ALU.mult).then_inc(y_final, 1)


SMALL_SCALES = 2 + 5 + 4 * 3 + 8


_INS = ["x", "adj", "L0_gnn_Wq", "L0_gnn_Wk", "L0_gnn_Wv", "L0_gnn_Wout"]
_OUTS = [((2048, 256), "float32")]


def kernel(**inputs):
    import numpy as _np
    import concourse.bacc as _bacc
    from concourse import mybir as _mybir
    from concourse.bass_utils import run_bass_kernel_spmd as _run

    nc = _bacc.Bacc("TRN2", target_bir_lowering=False, num_devices=1)
    arrays, args = {}, []
    for name in _INS:
        arr = _np.ascontiguousarray(inputs[name])
        arrays[f"in_{name}_dram"] = arr
        args.append(nc.dram_tensor(f"in_{name}_dram", arr.shape, _mybir.dt.from_np(arr.dtype), kind="ExternalInput").ap())
    for i, (shape, dtype) in enumerate(_OUTS):
        dt = _mybir.dt.from_np(_np.dtype(dtype))
        args.append(nc.dram_tensor(f"out_{i}_dram", shape, dt, kind="ExternalOutput").ap())
    preln_graph_attention(nc, *args)
    r = _run(nc, [arrays], core_ids=[0])
    return r.results[0]["out_0_dram"]
```

```python
import concourse.bass as bass
from concourse import mybir
import math
from contextlib import ExitStack


def preln_graph_attention(nc, x, adj, wq, wk, wv, wout, out):
    f32, f16, i32 = mybir.dt.float32, mybir.dt.float16, mybir.dt.int32
    ALU = mybir.AluOpType
    ACT = mybir.ActivationFunctionType
    AX = mybir.AxisListType
    RED = bass.bass_isa.ReduceOp
    ds = bass.ds

    P = 128
    N, D = x.shape
    H = wq.shape[1] // D
    R = N // H
    KC = D // P
    T = N // P
    CP = H // 2
    BANK = 512
    HALF = N // 2
    XT_GROUPS = KC * N // BANK
    UNITS = 4 * KC * CP
    USES = UNITS + 4 * T
    MASKED = -3.0e38
    REF_MASK = -1.0e6
    P_SCALE = 32768.0
    LN_P_SCALE = math.log(P_SCALE)
    EPS = 1e-5
    SCALE_INV = float(D) ** 0.5

    adj_t = adj.rearrange("(u r c) m -> c u r m", u=2, c=H)
    x_t = x.rearrange("(u r c) d -> u r c d", u=2, c=H)
    out_t = out.rearrange("(u r c) d -> c u r d", u=2, c=H)
    bias_dram = nc.dram_tensor("bias_dram", [T // 2, 2, P, N], f32, kind="Internal").ap()
    wo_dram = nc.dram_tensor("wo_dram", [P, 2, T, D], f16, kind="Internal").ap()

    ctx = ExitStack()
    with ctx:
        def sb(name, shape, dt):
            return ctx.enter_context(nc.sbuf_tensor(name, shape, dt))

        def sem(name):
            return ctx.enter_context(nc.semaphore(name))

        w_hi = [sb(f"w{n}_hi", [P, KC, H * D], f16) for n in "qkv"]
        w_lo = [sb(f"w{n}_lo", [P, KC, H * D], f16) for n in "qkv"]
        wo = sb("wo", [P, 2, KC, D], f16)
        xT_hi = sb("xT_hi", [P, KC, N], f16)
        xT_lo = sb("xT_lo", [P, KC, N], f16)
        qT = sb("qT", [P, 2, KC, N], f16)
        kT_f = sb("kT", [P, KC * N], f32)
        kT = kT_f.bitcast(f16)[:, :].rearrange("p (s k n) -> p s k n", s=2, k=KC)
        x_nat = kT_f[:, :].rearrange("p (t d) -> p t d", d=D)
        vw_f = sb("vw", [P, T * D], f32)
        vw = vw_f.bitcast(f16)[:, :].rearrange("p (t s d) -> p t s d", s=2, d=D)
        vT = sb("vT", [P, 2, 2, KC, BANK], f16)
        y = sb("y", [P, T, D], f32)
        a = sb("a", [P, 2, N], f32)
        bias = sb("bias", [P, 2, N], f32)
        p_raw = sb("p_raw", [P, 2 * N], f32)
        p_hi = p_raw.bitcast(f16)[:, 0:N]
        p_lo = p_raw.bitcast(f16)[:, N:2 * N]
        raw = p_raw[:, N:2 * N]
        pT = sb("pT", [P, 2, 2, T, P], f16)
        mask = sb("mask", [P, N], mybir.dt.uint8)
        ident = sb("ident", [P, P], f32)
        stats = sb("stats", [P, T, 6], f32)
        mv = sb("mv", [P, T, 2], f32)
        var_e = sb("var_e", [P, T], f32)
        std = sb("std", [P, T], f32)
        rstd = sb("rstd", [P, T], f32)
        newton = sb("newton", [P, T], f32)
        wmax = sb("wmax", [P, 4], f32)
        wall = sb("wall", [P, 4], f32)
        wscale = sb("wscale", [P, 4], f32)
        s_score = sb("s_score", [P, 1], f32)
        s_bias = sb("s_bias", [P, 1], f32)
        kappa = sb("kappa", [P, 1], f32)
        neg_kappa = sb("neg_kappa", [P, 1], f32)
        floor0 = sb("floor0", [P, 1], f32)
        s_out = sb("s_out", [P, 1], f32)
        s_out_inv = sb("s_out_inv", [P, 1], f32)
        ref_mask = sb("ref_mask", [P, 1], f32)
        n_masked = sb("n_masked", [P, T], f32)
        floor_a = sb("floor_a", [P, T], f32)
        floor = sb("floor", [P, T], f32)
        half_max = sb("half_max", [P, 2, 2], f32)
        row_max = sb("row_max", [P, 2], f32)
        shift = sb("shift", [P, 2], f32)
        row_sum = sb("row_sum", [P, 2], f32)
        mask_exp = sb("mask_exp", [P, 2], f32)
        denom = sb("denom", [P, 2], f32)
        rdenom = sb("rdenom", [P, T], f32)

        stage = [vw_f[:, :], a[:, :, :].rearrange("p u n -> p (u n)"),
                 bias[:, :, :].rearrange("p u n -> p (u n)"), p_raw[:, :]]
        wo_split = pT[:, :, :, :, :].rearrange("p u s t n -> p u (s t n)")
        split_hi = [w[:, :, :].rearrange("p k n -> p (k n)") for w in w_hi] + [wo_split[:, 0, :]]
        split_lo = [w[:, :, :].rearrange("p k n -> p (k n)") for w in w_lo] + [wo_split[:, 1, :]]

        work = ctx.enter_context(nc.psum_tensor("work", [P, 4, BANK], f32))
        turn = ctx.enter_context(nc.psum_tensor("turn", [P, 2, BANK], f32))
        yps = ctx.enter_context(nc.psum_tensor("yps", [P, 2, BANK], f32))

        x_loaded = [sem(f"x_loaded{q}") for q in range(4)]
        w_loaded = [sem(f"w_loaded{n}") for n in "qkvo"]
        xres_loaded = sem("xres_loaded")
        ident_set = sem("ident_set")
        wmax_ready = sem("wmax_ready")
        wall_ready = sem("wall_ready")
        wscale_ready = sem("wscale_ready")
        w_hi_ready = sem("w_hi_ready")
        w_split = [sem(f"w_split{n}") for n in "qkvo"]
        small = sem("small")
        var_ready = sem("var_ready")
        std_ready = sem("std_ready")
        x_normed = sem("x_normed")
        x_turned = sem("x_turned")
        xT_hi_ready = sem("xT_hi_ready")
        xT_split = sem("xT_split")
        wo_stored = sem("wo_stored")
        wo_loaded = sem("wo_loaded")
        bank_filled = sem("bank_filled")
        bank_free = sem("bank_free")
        unit_hi = sem("unit_hi")
        shift_ready = sem("shift_ready")
        bias_used = sem("bias_used")
        denom_ready = sem("denom_ready")
        p_hi_ready = sem("p_hi_ready")
        p_split = sem("p_split")
        p_turned = [sem(f"p_turned{u}") for u in range(2)]
        denom_summed = sem("denom_summed")
        rdenom_ready = sem("rdenom_ready")
        turn_steps = sem("turn_steps")
        y_filled = sem("y_filled")
        y_free = sem("y_free")
        y_chain = sem("y_chain")
        y_final = sem("y_final")
        raw_loaded = sem("raw_loaded")
        mask_made = sem("mask_made")
        adj_scaled = sem("adj_scaled")
        bias_made = sem("bias_made")
        floor_made = sem("floor_made")
        bias_stored = [sem(f"bias_stored{u}") for u in range(2)]
        bias_loaded = [sem(f"bias_loaded{u}") for u in range(2)]
        out_stored = sem("out_stored")

        QK = 2 * KC * CP
        VF = [("V", 0), ("V", 1), ("F", 0), ("V", 2), ("F", 1), ("V", 3), ("F", 2), ("F", 3)]
        VF_USE = QK + 4
        VF_POS = {kind_pair: 2 * n for n, kind_pair in enumerate(VF)}

        def score_use(h, t):
            return USES * h + QK if isinstance(t, int) and t == 0 else USES * h + UNITS + 4 * t

        block = ctx.enter_context(nc.Block())

        @block.sync
        def _(sp):
            for q in range(4):
                sp.dma_start(x_nat[:, 4 * q:4 * q + 4, :], x[4 * P * q:4 * P * q + 4 * P, :]
                             .rearrange("(t p) d -> p t d", p=P)).then_inc(x_loaded[q], 16)
            for n, w in ((0, wq), (1, wk), (3, wout), (2, wv)):
                if n == 3:
                    sp.dma_start(stage[3].rearrange("p (t d) -> p t d", d=D),
                                 w.rearrange("(t p) d -> p t d", p=P)).then_inc(w_loaded[3], 16)
                else:
                    sp.dma_start(stage[n].rearrange("p (k n) -> p k n", k=KC),
                                 w.rearrange("(k p) n -> p k n", p=P)).then_inc(w_loaded[n], 16)
            for u in range(2):
                sp.dma_start(y[:, u:T:2, :], x_t[u]).then_inc(xres_loaded, 16)

            def turn_hi(made, applied, u):
                sp.wait_ge(p_hi_ready, made)
                sp.sem_inc(turn_steps, 1)
                if applied is not None:
                    sp.wait_ge(y_filled, applied)
                    sp.sem_inc(turn_steps, 1)
                sp.dma_start_transpose(pT[:, u, 0, :, :], p_hi).then_inc(p_turned[u], 16)

            def turn_lo(made, u):
                sp.wait_ge(p_split, made)
                sp.sem_inc(turn_steps, 1)
                sp.dma_start_transpose(pT[:, u, 1, :, :], p_lo).then_inc(p_turned[u], 16)

            def load_raw(c, u, n):
                sp.wait_ge(mask_made, n)
                sp.wait_ge(adj_scaled, n)
                sp.dma_start(raw, adj_t[ds(c, 1), u].rearrange("o r m -> (o r) m")).then_inc(raw_loaded, 16)

            sp.wait_ge(w_split[3], 1)
            sp.dma_start(raw, adj_t[0, 0]).then_inc(raw_loaded, 16)
            load_raw(0, 1, 1)
            sp.wait_ge(wo_stored, 16)
            for u in range(2):
                turn_hi(u + 1, None, u)
                load_raw(1, u, u + 2)
                turn_lo(u + 1, u)
            with sp.Fori(1, T // 2 - 1) as j:
                counts = [(sp.snap(2 * j + u + 1), sp.snap(2 * j + u - 1)) for u in range(2)]
                for u in range(2):
                    load_raw(j + 1, u, 2 * j + u + 2)
                    turn_hi(*counts[u], u)
                    turn_lo(counts[u][0], u)
            with sp.Fori(T // 2 - 1, H * T // 2) as j:
                counts = [(sp.snap(2 * j + u + 1), sp.snap(2 * j + u - 1)) for u in range(2)]
                for u in range(2):
                    turn_hi(*counts[u], u)
                    turn_lo(counts[u][0], u)

        @block.gpsimd
        def _(pool):
            pool.memset(ident[:, :], 0.0).then_inc(ident_set, 1)
            pool.memset(ref_mask[:, :], REF_MASK).then_inc(ident_set, 1)
            pool.wait_ge(ident_set, 2)
            pool.affine_select(out=ident[:, :], in_=ident[:, :], compare_op=ALU.not_equal, fill=1.0, base=0,
                               pattern=[[-1, P]], channel_multiplier=1).then_inc(ident_set, 1)
            for i, n in enumerate((0, 1, 3, 2)):
                pool.wait_ge(wmax_ready, i + 1)
                pool.partition_all_reduce(wall[:, n:n + 1], wmax[:, n:n + 1], P, RED.max).then_inc(wall_ready, 1)
            pool.wait_ge(xres_loaded, 32)
            pool.wait_ge(small, SMALL_SCALES)
            pool.tensor_scalar(y[:, :, :].rearrange("p t d -> p (t d)"), y[:, :, :].rearrange("p t d -> p (t d)"),
                               s_out[:, 0:1], None, ALU.mult).then_inc(y_chain, 1)
            pool.wait_ge(w_split[3], 1)
            pool.dma_start(wo_dram[:, :, :, :], wo_split.rearrange("p s (t d) -> p s t d", d=D)).then_inc(wo_stored, 16)
            pool.wait_ge(wo_stored, 16)
            pool.dma_start(wo[:, :, :, :], wo_dram[:, :, 0:KC, :]).then_inc(wo_loaded, 16)

            def store_bias(c, u, made):
                pool.wait_ge(bias_made, made)
                pool.dma_start(bias_dram[ds(c, 1), u].rearrange("o p m -> (o p) m"),
                               bias[:, u, :]).then_inc(bias_stored[u], 16)

            def lo_part(t, u):
                pool.wait_ge(p_hi_ready, t + 1)
                pool.tensor_tensor(p_lo, a[:, u, :], p_hi, ALU.subtract).then_inc(p_split, 1)

            store_bias(0, 0, 1)
            with pool.Fori(0, T // 2 - 1) as c:
                lo_part(2 * c, 0)
                store_bias(c, 1, 2 * c + 2)
                lo_part(2 * c + 1, 1)
                store_bias(c + 1, 0, 2 * c + 3)
            lo_part(T - 2, 0)
            store_bias(T // 2 - 1, 1, T)
            lo_part(T - 1, 1)

            with pool.Fori(1, H) as h:
                pool.wait_ge(bank_free, USES * (h - 1) + VF_USE + 2 * len(VF) + 4)
                pool.dma_start(wo[:, :, :, :], wo_dram[:, :, ds(KC * h, KC), :]).then_inc(wo_loaded, 16)

            with pool.Fori(0, T // 2) as c:
                for u in range(2):
                    pool.wait_ge(y_final, 2 * c + u + 1)
                    pool.dma_start(out_t[ds(c, 1), u].rearrange("o r d -> (o r) d"),
                                   y[:, ds(2 * c + u, 1), :].rearrange("p o d -> p (o d)")).then_inc(out_stored, 16)
            pool.wait_ge(out_stored, 16 * T)
            for u in range(2):
                pool.wait_ge(bias_stored[u], 16 * (T // 2))

        @block.tensor
        def _(pe):
            pe.wait_ge(ident_set, 3)
            for q in range(N // BANK):
                for k in range(KC):
                    n = KC * q + k
                    pe.wait_ge(x_normed, 4 * q + 4)
                    if n >= 2:
                        pe.wait_ge(xT_split, n - 1)
                    for j in range(4):
                        last = pe.transpose(turn[:, n % 2, P * j:P * j + P], x_nat[:, 4 * q + j, P * k:P * k + P],
                                            ident[:, :])
                    last.then_inc(x_turned, 1)

            def project(bank, w, d0, x0):
                for cc in range(2):
                    o = work[:, bank, R * cc:R * cc + R]
                    for k in range(KC):
                        hi = w_hi[w][:, k, ds(d0 + D * cc, P)]
                        lo = w_lo[w][:, k, ds(d0 + D * cc, P)]
                        pe.matmul(o, hi, xT_hi[:, k, ds(x0, R)], start=(k == 0), stop=False)
                        pe.matmul(o, hi, xT_lo[:, k, ds(x0, R)], start=False, stop=False)
                        last = pe.matmul(o, lo, xT_hi[:, k, ds(x0, R)], start=False, stop=(k == KC - 1))
                last.then_inc(bank_filled, 1)

            def fold(bank, slot, pair):
                for m in range(2):
                    o = work[:, bank, D * m:D * m + D]
                    c0 = P * (2 * pair + m)
                    for k in range(KC):
                        hi = vT[:, slot, 0, k, c0:c0 + P]
                        lo = vT[:, slot, 1, k, c0:c0 + P]
                        pe.matmul(o, hi, wo[:, 0, k, :], start=(k == 0), stop=False)
                        pe.matmul(o, hi, wo[:, 1, k, :], start=False, stop=False)
                        last = pe.matmul(o, lo, wo[:, 0, k, :], start=False, stop=(k == KC - 1))
                last.then_inc(bank_filled, 1)

            def project_qk_pair(h, cp):
                for w in range(2):
                    for dc in range(KC):
                        n = KC * w + dc
                        pe.wait_ge(bank_free, USES * h + 4 * cp + n + 1)
                        project(n, w, 2 * D * cp + P * dc, R * h)

            def project_qk(h, start):
                with pe.Fori(start, CP) as cp:
                    project_qk_pair(h, cp)

            def project_v(h):
                use = USES * h + VF_USE
                for kind, cp in VF:
                    for s in range(2):
                        i = VF_POS[kind, cp] + s
                        pe.wait_ge(bank_free, use + i + 1)
                        if kind == "V":
                            project(i % 4, 2, 2 * D * cp + P * s, R * h)
                        else:
                            if cp == 0 and s == 0:
                                pe.wait_ge(wo_loaded, 16 * h + 16)
                            pe.wait_ge(bank_free, use + VF_POS["V", cp] + 2 + 4)
                            fold(i % 4, cp % 2, s)

            def scores(h, t):
                for half in range(2):
                    use = score_use(h, t) + 2 * half
                    pe.wait_ge(bank_free, use + (4 if isinstance(t, int) and t == 0 and half == 0 else 2))
                    for b in range(2 * half, 2 * half + 2):
                        cols = slice(BANK * b, BANK * b + BANK)
                        for k in range(KC):
                            hi, lo = qT[:, 0, k, ds(P * t, P)], qT[:, 1, k, ds(P * t, P)]
                            pe.matmul(work[:, b, :], hi, kT[:, 0, k, cols], start=(k == 0), stop=False)
                            pe.matmul(work[:, b, :], hi, kT[:, 1, k, cols], start=False, stop=False)
                            last = pe.matmul(work[:, b, :], lo, kT[:, 0, k, cols], start=False, stop=(k == KC - 1))
                        last.then_inc(bank_filled, 1)

            def apply(h, i, u):
                pe.wait_ge(y_free, T * h + 2 * i + u + 1)
                pe.wait_ge(p_turned[u], 32 * (T // 2 * h + i) + 32)
                for m in range(T):
                    pe.matmul(yps[:, u, :], pT[:, u, 0, m, :], vw[:, m, :, :].rearrange("p s d -> p (s d)"),
                              start=(m == 0), stop=False)
                    last = pe.matmul(yps[:, u, D:2 * D], pT[:, u, 1, m, :], vw[:, m, 0, :],
                                     start=False, stop=(m == T - 1))
                last.then_inc(y_filled, 1)

            def head(h, last):
                with pe.Fori(0, T // 2 - 1) as i:
                    for u in range(2):
                        scores(h, 2 * i + u + 2)
                        apply(h, i, u)
                if not last:
                    project_qk_pair(h + 1, 0)
                apply(h, T // 2 - 1, 0)
                if not last:
                    project_qk(h + 1, 1)
                apply(h, T // 2 - 1, 1)
                if not last:
                    scores(h + 1, 0)
                    project_v(h + 1)
                    scores(h + 1, 1)

            pe.wait_ge(w_split[0], 1)
            pe.wait_ge(w_split[1], 1)
            pe.wait_ge(xT_split, XT_GROUPS)
            project_qk(0, 0)
            scores(0, 0)
            pe.wait_ge(w_split[2], 1)
            project_v(0)
            scores(0, 1)
            head(0, False)
            with pe.Fori(1, H - 1) as h:
                head(h, False)
            head(H - 1, True)

        @block.scalar
        def _(act):
            act.wait_ge(var_ready, 1)
            act.activation(std[:, :], var_e[:, :], ACT.Sqrt).then_inc(std_ready, 1)

            def w_part(n, count):
                act.wait_ge(wscale_ready, count)
                act.activation(split_hi[n], stage[n], ACT.Copy, scale=wscale[:, n:n + 1]).then_inc(w_hi_ready, 1)

            w_part(0, 1)
            for g in range(XT_GROUPS):
                if g == 2:
                    w_part(1, 2)
                q, k = g // KC, g % KC
                act.wait_ge(x_turned, g + 1)
                act.activation(xT_hi[:, k, BANK * q:BANK * q + BANK], turn[:, g % 2, :], ACT.Relu
                               ).then_inc(xT_hi_ready, 1)

            def bias_tile(t, u, i=None):
                act.wait_ge(raw_loaded, 16 * (t + 1))
                if i is not None:
                    act.wait_ge(bias_stored[u], 16 * i + 16)
                    act.wait_ge(bias_used, t - 1)
                act.activation(bias[:, u, :].rearrange("p (c r) -> p c r", c=H),
                               raw.rearrange("p (r c) -> p c r", c=H), ACT.Copy,
                               scale=s_bias[:, 0:1]).then_inc(adj_scaled, 1)

            def unit(use, dst, bank, scale):
                act.wait_ge(bank_filled, use + 1)
                act.activation(dst, bank, ACT.Copy, scale=scale).then_inc(unit_hi, 1)

            def exp(h, t, u):
                act.wait_ge(shift_ready, T * h + t + 1)
                act.activation(a[:, u, :], a[:, u, :], ACT.Exp, bias=shift[:, u:u + 1], scale=kappa[:, 0:1],
                               accum_out=row_sum[:, u:u + 1])
                act.activation(mask_exp[:, u:u + 1], shift[:, u:u + 1], ACT.Exp, bias=ref_mask[:, 0:1],
                               scale=1.0).then_inc(denom_ready, 1)

            def split_p(h, t, i, u):
                act.wait_ge(denom_ready, T * h + t + 1)
                if not (isinstance(h, int) and h == 0 and isinstance(t, int) and t == 0):
                    act.wait_ge(p_turned[1 - u], 32 * (T // 2 * h + i + u))
                act.activation(p_hi, a[:, u, :], ACT.Copy).then_inc(p_hi_ready, 1)

            def load_bias(c, u):
                act.dma_start(bias[:, u, :], bias_dram[ds(c, 1), u].rearrange("o p m -> (o p) m")
                              ).then_inc(bias_loaded[u], 16)

            def units_qk_pair(h, cp):
                for w, dst in ((0, qT), (1, kT)):
                    for dc in range(KC):
                        n = KC * w + dc
                        unit(USES * h + 4 * cp + n, dst[:, 0, dc, ds(BANK * cp, BANK)], work[:, n, :], 1.0)

            def units_qk(h):
                with act.Fori(0, CP) as cp:
                    units_qk_pair(h, cp)

            def units_v(h, some):
                for kind, cp in some:
                    for s in range(2):
                        i = VF_POS[kind, cp] + s
                        bank = work[:, i % 4, :]
                        if kind == "V":
                            unit(USES * h + VF_USE + i, vT[:, cp % 2, 0, s, :], bank, 1.0)
                        else:
                            t0 = 4 * cp + 2 * s
                            unit(USES * h + VF_USE + i, vw[:, t0:t0 + 2, 0, :],
                                 bank.rearrange("p (t d) -> p t d", d=D), 1.0 / P_SCALE)

            def two_tiles(h, i, first, last):
                for u in range(2):
                    t = 2 * i + u + 2
                    exp(h, t, u)
                    if first and not (isinstance(i, int) and u == 1):
                        bias_tile(t + 1, 1 - u, i + u)
                    if isinstance(i, int):
                        if not last:
                            if first:
                                act.wait_ge(bias_stored[u], 16 * (T // 2))
                            load_bias(0, u)
                    elif not first:
                        load_bias(i + 2, u)
                    split_p(h, t, i + 1, u)

            def start_head(h, first):
                if not first:
                    units_qk(h)
                units_v(h, VF[0:1])
                exp(h, 0, 0)
                if not first:
                    load_bias(1, 0)
                units_v(h, VF[1:2])
                split_p(h, 0, 0, 0)
                units_v(h, VF[2:])
                if first:
                    bias_tile(1, 1)
                exp(h, 1, 1)
                if first:
                    bias_tile(2, 0, 0)
                else:
                    load_bias(1, 1)
                split_p(h, 1, 0, 1)

            def head(h, first, last):
                with act.Fori(0, T // 2 - 2) as i:
                    two_tiles(h, i, first, last)
                two_tiles(h, T // 2 - 2, first, last)
                if not last:
                    start_head(h + 1, False)

            units_qk_pair(0, 0)
            units_qk_pair(0, 1)
            w_part(3, 3)
            units_qk_pair(0, 2)
            w_part(2, 4)
            units_qk_pair(0, 3)
            act.wait_ge(small, SMALL_SCALES)
            act.wait_ge(w_split[2], 1)
            bias_tile(0, 0)
            start_head(0, True)
            head(0, True, False)
            with act.Fori(1, H - 1) as h:
                head(h, False, False)
            head(H - 1, False, True)

        @block.vector
        def _(dve):
            dve.nop().then_inc(bank_free, 4)
            dve.nop().then_inc(y_free, 2)
            chain = [0]

            def link(ins):
                chain[0] += 1
                ins.then_inc(small, 1)
                dve.wait_ge(small, chain[0])

            for t in range(T):
                if t % 4 == 0:
                    dve.wait_ge(x_loaded[t // 4], 16)
                last = dve.bn_stats(stats[:, t, :], x_nat[:, t, :])
            link(last)
            for t in range(T):
                last = dve.bn_aggr(mv[:, t, :], stats[:, t, :])
            link(last)
            dve.tensor_scalar(var_e[:, :], mv[:, :, 1], EPS, None, ALU.add).then_inc(var_ready, 1)

            def w_max(n):
                dve.wait_ge(w_loaded[n], 16)
                dve.tensor_reduce(wmax[:, n:n + 1], stage[n], AX.X, ALU.max, apply_absolute_value=True
                                  ).then_inc(wmax_ready, 1)

            w_max(0)
            dve.wait_ge(std_ready, 1)
            link(dve.reciprocal(rstd[:, :], std[:, :]))
            link(dve.tensor_tensor(newton[:, :], rstd[:, :], rstd[:, :], ALU.mult))
            link(dve.tensor_tensor(newton[:, :], newton[:, :], var_e[:, :], ALU.mult))
            link(dve.tensor_scalar(newton[:, :], newton[:, :], -0.5, 1.5, ALU.mult, ALU.add))
            link(dve.tensor_tensor(rstd[:, :], rstd[:, :], newton[:, :], ALU.mult))
            for t in range(T):
                dve.tensor_scalar(x_nat[:, t, :], x_nat[:, t, :], mv[:, t, 0:1], rstd[:, t:t + 1],
                                  ALU.subtract, ALU.mult).then_inc(x_normed, 1)

            def scale_of(n, count):
                dve.wait_ge(wall_ready, count)
                s = wscale[:, n:n + 1]
                link(dve.tensor_scalar(s, wall[:, n:n + 1], LEAST[n], None, ALU.max))
                link(dve.tensor_scalar(s.bitcast(i32), s.bitcast(i32), 0x7f800000, None, ALU.bitwise_and))
                link(dve.reciprocal(s, s))
                dve.tensor_scalar(s, s, 64.0, None, ALU.mult).then_inc(wscale_ready, 1)

            def split_w(n, count):
                dve.wait_ge(w_hi_ready, count)
                dve.scalar_tensor_tensor(out=split_lo[n], in0=stage[n], scalar=wscale[:, n:n + 1], in1=split_hi[n],
                                         op0=ALU.mult, op1=ALU.subtract).then_inc(w_split[n], 1)

            LEAST = [2.0 ** -20, 2.0 ** -20, 2.0 ** -30, 2.0 ** -30]
            scale_of(0, 1)
            w_max(1)
            scale_of(1, 2)
            for g in range(XT_GROUPS):
                q, k = g // KC, g % KC
                dve.wait_ge(xT_hi_ready, g + 1)
                dve.scalar_tensor_tensor(out=xT_lo[:, k, BANK * q:BANK * q + BANK], in0=turn[:, g % 2, :], scalar=0.0,
                                         in1=xT_hi[:, k, BANK * q:BANK * q + BANK], op0=ALU.max, op1=ALU.subtract
                                         ).then_inc(xT_split, 1)
                if g == 1:
                    split_w(0, 1)
                if g == 3:
                    split_w(1, 2)
            def unit(count, dst, bank, hi, scale):
                dve.wait_ge(unit_hi, count)
                if scale == 1.0:
                    dve.tensor_tensor(dst, bank, hi, ALU.subtract).then_inc(bank_free, 1)
                else:
                    dve.scalar_tensor_tensor(out=dst, in0=bank, scalar=scale, in1=hi, op0=ALU.mult,
                                             op1=ALU.subtract).then_inc(bank_free, 1)

            def units_qk_pair(h, cp):
                for w, dst in ((0, qT), (1, kT)):
                    for dc in range(KC):
                        n = KC * w + dc
                        cols = ds(BANK * cp, BANK)
                        unit(UNITS * h + 4 * cp + n + 1, dst[:, 1, dc, cols], work[:, n, :], dst[:, 0, dc, cols], 1.0)

            w_max(3)
            units_qk_pair(0, 0)
            w_max(2)
            units_qk_pair(0, 1)
            scale_of(3, 3)
            scale_of(2, 4)
            dve.wait_ge(wscale_ready, 4)
            link(dve.tensor_tensor(s_score[:, :], wscale[:, 0:1], wscale[:, 1:2], ALU.mult))
            link(dve.tensor_scalar(s_score[:, :], s_score[:, :], SCALE_INV, None, ALU.mult))
            link(dve.tensor_scalar(s_bias[:, :], s_score[:, :], 2.0, None, ALU.mult))
            link(dve.tensor_scalar(floor0[:, :], s_score[:, :], REF_MASK, None, ALU.mult))
            link(dve.reciprocal(kappa[:, :], s_score[:, :]))
            link(dve.tensor_scalar(neg_kappa[:, :], kappa[:, :], -1.0, None, ALU.mult))
            link(dve.tensor_tensor(s_out[:, :], wscale[:, 2:3], wscale[:, 3:4], ALU.mult))
            link(dve.tensor_scalar(s_out[:, :], s_out[:, :], 1.0 / P_SCALE, None, ALU.mult))
            link(dve.reciprocal(s_out_inv[:, :], s_out[:, :]))
            assert chain[0] == SMALL_SCALES

            def mask_tile(t):
                dve.wait_ge(raw_loaded, 16 * (t + 1))
                if not (isinstance(t, int) and t == 0):
                    dve.wait_ge(bias_made, t)
                dve.tensor_scalar(mask[:, :], raw, 0.0, 0.0, ALU.is_equal, ALU.add,
                                  accum_out=n_masked[:, ds(t, 1)]).then_inc(mask_made, 1)

            def bias_tile(t, u):
                col = ds(t, 1)
                dve.wait_ge(mask_made, t + 1)
                dve.wait_ge(adj_scaled, t + 1)
                dve.scalar_tensor_tensor(out=bias[:, u, :].rearrange("p (c r) -> p c r", c=H),
                                         in0=mask[:, :].rearrange("p (r c) -> p c r", c=H), scalar=MASKED,
                                         in1=bias[:, u, :].rearrange("p (c r) -> p c r", c=H),
                                         op0=ALU.mult, op1=ALU.add).then_inc(bias_made, 1)
                dve.tensor_scalar(floor_a[:, col], n_masked[:, col], 0.0, MASKED, ALU.is_equal, ALU.mult
                                  ).then_inc(floor_made, 1)
                dve.wait_ge(floor_made, 2 * t + 1)
                dve.tensor_scalar(floor[:, col], floor_a[:, col], floor0[:, 0:1], None, ALU.add
                                  ).then_inc(floor_made, 1)

            def units_qk(h):
                with dve.Fori(1, CP) as cp:
                    units_qk_pair(h, cp)

            def units_v(h, some):
                for kind, cp in some:
                    for s in range(2):
                        i = VF_POS[kind, cp] + s
                        count = UNITS * h + QK + i + 1
                        bank = work[:, i % 4, :]
                        if kind == "V":
                            unit(count, vT[:, cp % 2, 1, s, :], bank, vT[:, cp % 2, 0, s, :], 1.0)
                        else:
                            t0 = 4 * cp + 2 * s
                            unit(count, vw[:, t0:t0 + 2, 1, :], bank.rearrange("p (t d) -> p t d", d=D),
                                 vw[:, t0:t0 + 2, 0, :], 1.0 / P_SCALE)

            def softmax_shift(h, t, i, u, first):
                use = score_use(h, t)
                if first:
                    dve.wait_ge(bias_made, t + 1)
                    dve.wait_ge(floor_made, 2 * t + 2)
                    if not (isinstance(t, int) and t < 2):
                        dve.wait_ge(p_split, t - 1)
                else:
                    dve.wait_ge(bias_loaded[u], 16 * (T // 2) * (h - 1) + 16 * i + 16)
                for half in range(2):
                    dve.wait_ge(bank_filled, use + 2 * half + 2)
                    cols = slice(HALF * half, HALF * half + HALF)
                    dve.tensor_tensor_reduce(a[:, u, cols],
                                             work[:, 2 * half:2 * half + 2, :].rearrange("p b n -> p (b n)"),
                                             bias[:, u, cols], 1.0, MASKED, ALU.add, ALU.max,
                                             half_max[:, u, half:half + 1]).then_inc(bank_free, 2)
                dve.wait_ge(bank_free, use + 4 + 4)
                dve.tensor_scalar(row_max[:, u:u + 1], half_max[:, u, 0:1], half_max[:, u, 1:2],
                                  floor[:, ds(t, 1)], ALU.max, ALU.max).then_inc(bias_used, 1)
                dve.wait_ge(bias_used, T * h + t + 1)
                dve.tensor_scalar(shift[:, u:u + 1], row_max[:, u:u + 1], neg_kappa[:, 0:1], LN_P_SCALE,
                                  ALU.mult, ALU.add).then_inc(shift_ready, 1)

            def split_p(h, t, u, first):
                g = T * h + t
                if not first:
                    dve.wait_ge(p_hi_ready, g + 1)
                    dve.tensor_tensor(p_lo, a[:, u, :], p_hi, ALU.subtract).then_inc(p_split, 1)
                dve.wait_ge(denom_ready, g + 1)
                dve.scalar_tensor_tensor(out=denom[:, u:u + 1], in0=mask_exp[:, u:u + 1], scalar=n_masked[:, ds(t, 1)],
                                         in1=row_sum[:, u:u + 1], op0=ALU.mult, op1=ALU.add).then_inc(denom_summed, 1)
                dve.wait_ge(denom_summed, g + 1)
                dve.reciprocal(rdenom[:, ds(t, 1)], denom[:, u:u + 1]).then_inc(rdenom_ready, 1)

            def update_y(h, t, u, last):
                g = T * h + t
                yt = y[:, ds(t, 1), :].rearrange("p o d -> p (o d)")
                r = rdenom[:, ds(t, 1)]
                dve.wait_ge(rdenom_ready, g + 1)
                dve.wait_ge(y_filled, g + 1)
                dve.scalar_tensor_tensor(out=yt, in0=yps[:, u, 0:D], scalar=r, in1=yt,
                                         op0=ALU.mult, op1=ALU.add).then_inc(y_chain, 1)
                dve.wait_ge(y_chain, g + 2)
                dve.scalar_tensor_tensor(out=yt, in0=yps[:, u, D:2 * D], scalar=r, in1=yt,
                                         op0=ALU.mult, op1=ALU.add).then_inc(y_free, 1)
                if last:
                    dve.wait_ge(y_free, g + 3)
                    dve.tensor_scalar(yt, yt, s_out_inv[:, 0:1], None, ALU.mult).then_inc(y_final, 1)

            def start_head(h, first, second=False):
                if not first:
                    units_qk(h)
                    update_y(h - 1, T - 1, 1, False)
                if second:
                    dve.wait_ge(p_split, T)
                softmax_shift(h, 0, 0, 0, first)
                units_v(h, VF[0:2])
                if first:
                    mask_tile(1)
                split_p(h, 0, 0, first)
                units_v(h, VF[2:])
                if first:
                    bias_tile(1, 1)
                softmax_shift(h, 1, 0, 1, first)

            def head(h, first, last):
                with dve.Fori(0, T // 2 - 1) as i:
                    for u in range(2):
                        t = 2 * i + u
                        if first:
                            mask_tile(t + 2)
                        split_p(h, t + 1, 1 - u, first)
                        if first:
                            bias_tile(t + 2, u)
                        softmax_shift(h, t + 2, i + 1, u, first)
                        update_y(h, t, u, last)
                split_p(h, T - 1, 1, first)
                if not last:
                    units_qk_pair(h + 1, 0)
                update_y(h, T - 2, 0, last)
                if last:
                    update_y(h, T - 1, 1, last)
                else:
                    start_head(h + 1, False, first)

            units_qk_pair(0, 2)
            split_w(3, 3)
            units_qk_pair(0, 3)
            split_w(2, 4)
            mask_tile(0)
            bias_tile(0, 0)
            start_head(0, True)
            dve.wait_ge(y_chain, 1)
            head(0, True, False)
            with dve.Fori(1, H - 1) as h:
                head(h, False, False)
            head(H - 1, False, True)


SMALL_SCALES = 2 + 5 + 4 * 3 + 9


_INS = ["x", "adj", "L0_gnn_Wq", "L0_gnn_Wk", "L0_gnn_Wv", "L0_gnn_Wout"]
_OUTS = [((2048, 256), "float32")]


def kernel(**inputs):
    import numpy as _np
    import concourse.bacc as _bacc
    from concourse import mybir as _mybir
    from concourse.bass_utils import run_bass_kernel_spmd as _run

    nc = _bacc.Bacc("TRN2", target_bir_lowering=False, num_devices=1)
    arrays, args = {}, []
    for name in _INS:
        arr = _np.ascontiguousarray(inputs[name])
        arrays[f"in_{name}_dram"] = arr
        args.append(nc.dram_tensor(f"in_{name}_dram", arr.shape, _mybir.dt.from_np(arr.dtype), kind="ExternalInput").ap())
    for i, (shape, dtype) in enumerate(_OUTS):
        dt = _mybir.dt.from_np(_np.dtype(dtype))
        args.append(nc.dram_tensor(f"out_{i}_dram", shape, dt, kind="ExternalOutput").ap())
    preln_graph_attention(nc, *args)
    r = _run(nc, [arrays], core_ids=[0])
    return r.results[0]["out_0_dram"]
```
